# Optimizing a Trainium2 kernel written in Bass

```python
import numpy as np
import jax
import jax.numpy as jnp

def _softmax(x, axis=-1):
    return jax.nn.softmax(x, axis=axis)

def _gelu(x):
    return jax.nn.gelu(x, approximate=True)

def _silu(x):
    return jax.nn.silu(x)

def _sigmoid(x):
    return jax.nn.sigmoid(x)

def _layernorm(x, axis=-1, eps=1e-05):
    m = jnp.mean(x, axis=axis, keepdims=True)
    v = jnp.var(x, axis=axis, keepdims=True)
    return (x - m) / jnp.sqrt(v + eps)

def _scatter_add(tgt, idx, src, axis=0):
    return tgt.at[idx].add(src)

def _segment_sum(src, seg, n):
    return jax.ops.segment_sum(src, seg, n)
kernel_name = 'mk_adj_resnorm_d2_adj_r2_897307'

def setup_inputs(seed: int=0):
    np.random.seed(seed)
    _w = jnp.asarray

    def _rec_inputs():
        import jax
        import jax.numpy as jnp
        _gk = jax.random.key(seed)
        x = -0.000929 + 1 * jax.random.normal(jax.random.fold_in(_gk, 1), (4096, 128), jnp.float32)
        _a = jax.random.bernoulli(jax.random.fold_in(_gk, 2), 0.00195312, (4096, 4096))
        _a = jnp.logical_or(_a, jnp.eye(4096, dtype=bool))
        _af = _a.astype(jnp.float32)
        _af = _af * jax.random.uniform(jax.random.fold_in(_gk, 3), (4096, 4096), jnp.float32, 0.05, 1)
        adj = _af
        return (x, adj)
    x, adj = _rec_inputs()

    def _L0_gnn_setup():
        import jax, jax.numpy as jnp
        import numpy as np
        NEG_SLOPE = 0.01
        N_U, N_V = (4096, 4096)
        U_F, V_F = (128, 128)
        HIDS = [128, 128]
        NUM_ROUNDS = 3

        def _glorot(key, fan_in, fan_out):
            lim = np.sqrt(6.0 / (fan_in + fan_out)).astype(np.float32)
            return jax.random.uniform(key, (fan_in, fan_out), jnp.float32, -lim, lim)

        def _mlp(x, W1, b1, W2, b2, W3, b3):
            a = jax.nn.leaky_relu
            x = a(x @ W1 + b1, NEG_SLOPE)
            x = a(x @ W2 + b2, NEG_SLOPE)
            return a(x @ W3 + b3, NEG_SLOPE)
        key = jax.random.key(seed)
        ks = jax.random.split(key, 12)
        inp = {'u_node_feats': jax.random.normal(ks[0], (N_U, U_F), jnp.float32), 'v_node_feats': jax.random.normal(ks[1], (N_V, V_F), jnp.float32), 'uv_adj_mat': jax.random.uniform(ks[2], (N_V, N_U), jnp.float32), 'vu_adj_mat': jax.random.uniform(ks[3], (N_U, N_V), jnp.float32)}
        dims_uv = [U_F] + HIDS + [V_F]
        dims_vu = [V_F] + HIDS + [U_F]
        k = 4
        for tag, dims in (('uv', dims_uv), ('vu', dims_vu)):
            for i in range(3):
                inp[f'{tag}_W{i + 1}'] = _glorot(ks[k], dims[i], dims[i + 1])
                k += 1
                inp[f'{tag}_b{i + 1}'] = jnp.zeros((dims[i + 1],), jnp.float32)
        return inp
    _L0_gnn_all = _L0_gnn_setup()
    _L0_gnn_in = {k: v for k, v in _L0_gnn_all.items() if k in ('v_node_feats', 'uv_W1', 'uv_b1', 'uv_W2', 'uv_b2', 'uv_W3', 'uv_b3', 'vu_W1', 'vu_b1', 'vu_W2', 'vu_b2', 'vu_W3', 'vu_b3')}
    del _L0_gnn_all

    def _L1_gnn_setup():
        import jax, jax.numpy as jnp
        import numpy as np
        N = 5000
        IN_C = 128
        OUT_C = 128
        key = jax.random.key(seed)
        k1, k2, k3 = jax.random.split(key, 3)
        x = jax.random.normal(k1, (N, IN_C), dtype=jnp.float32)
        edge_index = jax.random.uniform(k2, (N, N), dtype=jnp.float32)
        limit = float(np.sqrt(6.0 / (IN_C + OUT_C)))
        weight = jax.random.uniform(k3, (IN_C, OUT_C), dtype=jnp.float32, minval=-limit, maxval=limit)
        return {'x': x, 'edge_index': edge_index, 'weight': weight}
    _L1_gnn_all = _L1_gnn_setup()
    _L1_gnn_in = {k: v for k, v in _L1_gnn_all.items() if k in ('weight',)}
    del _L1_gnn_all
    return {'x': x, 'adj': adj, 'L0_gnn_v_node_feats': _L0_gnn_in['v_node_feats'], 'L0_gnn_uv_W1': _L0_gnn_in['uv_W1'], 'L0_gnn_uv_b1': _L0_gnn_in['uv_b1'], 'L0_gnn_uv_W2': _L0_gnn_in['uv_W2'], 'L0_gnn_uv_b2': _L0_gnn_in['uv_b2'], 'L0_gnn_uv_W3': _L0_gnn_in['uv_W3'], 'L0_gnn_uv_b3': _L0_gnn_in['uv_b3'], 'L0_gnn_vu_W1': _L0_gnn_in['vu_W1'], 'L0_gnn_vu_b1': _L0_gnn_in['vu_b1'], 'L0_gnn_vu_W2': _L0_gnn_in['vu_W2'], 'L0_gnn_vu_b2': _L0_gnn_in['vu_b2'], 'L0_gnn_vu_W3': _L0_gnn_in['vu_W3'], 'L0_gnn_vu_b3': _L0_gnn_in['vu_b3'], 'L1_gnn_weight': _L1_gnn_in['weight']}

def reference(x, adj, L0_gnn_v_node_feats, L0_gnn_uv_W1, L0_gnn_uv_b1, L0_gnn_uv_W2, L0_gnn_uv_b2, L0_gnn_uv_W3, L0_gnn_uv_b3, L0_gnn_vu_W1, L0_gnn_vu_b1, L0_gnn_vu_W2, L0_gnn_vu_b2, L0_gnn_vu_W3, L0_gnn_vu_b3, L1_gnn_weight):
    import jax
    import jax.numpy as jnp

    def _L0_gnn_ref(u_node_feats, v_node_feats, uv_adj_mat, vu_adj_mat, uv_W1, uv_b1, uv_W2, uv_b2, uv_W3, uv_b3, vu_W1, vu_b1, vu_W2, vu_b2, vu_W3, vu_b3):
        import jax, jax.numpy as jnp
        import numpy as np
        NEG_SLOPE = 0.01
        N_U, N_V = (4096, 4096)
        U_F, V_F = (128, 128)
        HIDS = [128, 128]
        NUM_ROUNDS = 3

        def _glorot(key, fan_in, fan_out):
            lim = np.sqrt(6.0 / (fan_in + fan_out)).astype(np.float32)
            return jax.random.uniform(key, (fan_in, fan_out), jnp.float32, -lim, lim)

        def _mlp(x, W1, b1, W2, b2, W3, b3):
            a = jax.nn.leaky_relu
            x = a(x @ W1 + b1, NEG_SLOPE)
            x = a(x @ W2 + b2, NEG_SLOPE)
            return a(x @ W3 + b3, NEG_SLOPE)
        u, v = (u_node_feats, v_node_feats)
        for _ in range(NUM_ROUNDS):
            v = _mlp(uv_adj_mat @ u, uv_W1, uv_b1, uv_W2, uv_b2, uv_W3, uv_b3)
            u = _mlp(vu_adj_mat @ v, vu_W1, vu_b1, vu_W2, vu_b2, vu_W3, vu_b3)
        return v

    def _L1_gnn_ref(x, edge_index, weight):
        import jax, jax.numpy as jnp
        import numpy as np
        N = 5000
        IN_C = 128
        OUT_C = 128
        support = jnp.matmul(x, weight)
        output = jnp.matmul(edge_index, support)
        return output
    x = _layernorm(x + _L0_gnn_ref(x, L0_gnn_v_node_feats, adj, adj, L0_gnn_uv_W1, L0_gnn_uv_b1, L0_gnn_uv_W2, L0_gnn_uv_b2, L0_gnn_uv_W3, L0_gnn_uv_b3, L0_gnn_vu_W1, L0_gnn_vu_b1, L0_gnn_vu_W2, L0_gnn_vu_b2, L0_gnn_vu_W3, L0_gnn_vu_b3), axis=-1)
    x = _layernorm(x + _L1_gnn_ref(x, adj, L1_gnn_weight), axis=-1)
    return x

_drawn_inputs = setup_inputs


def setup_inputs(seed=0):
    import zlib

    import numpy as np

    out = dict(_drawn_inputs(seed))
    spreads = {'L0_gnn_uv_b1': (0.0, 0.1),
     'L0_gnn_uv_b2': (0.0, 0.1),
     'L0_gnn_uv_b3': (0.0, 0.1),
     'L0_gnn_vu_b1': (0.0, 0.1),
     'L0_gnn_vu_b2': (0.0, 0.1),
     'L0_gnn_vu_b3': (0.0, 0.1)}
    factors = {}
    for name, (base, spread) in spreads.items():
        noise = np.random.default_rng([zlib.crc32(name.encode()), seed]).standard_normal(out[name].shape)
        drawn = base * np.exp(spread * noise) if base else spread * noise
        out[name] = jnp.asarray(drawn.astype(out[name].dtype))
    for name, factor in factors.items():
        out[name] = (out[name] * factor).astype(out[name].dtype)
    return out
```

```python
from contextlib import ExitStack

import concourse.bass as bass
from concourse import mybir

F32 = mybir.dt.float32
F32R = mybir.dt.float32r
ALU = mybir.AluOpType
ACT = mybir.ActivationFunctionType

N = 4096
D = 128
CHUNK = 512
CHUNKS = N // CHUNK
BLOCKS = N // D
GROUPS = 8
PER_GROUP = BLOCKS // GROUPS
GROUP = PER_GROUP * CHUNK
SLOTS = 4
LEAD = SLOTS - 1
ROUND_TRIPS = 2
PRODUCTS = 2 * ROUND_TRIPS + 2
STEPS = PRODUCTS * CHUNKS
NORM_STEP = (PRODUCTS - 2) * CHUNKS
LAST_STEP = (PRODUCTS - 1) * CHUNKS
SLOPE = 0.01
EPS = 1e-5

WEIGHTS = ["uv_W1", "uv_W2", "uv_W3", "vu_W1", "vu_W2", "vu_W3", "gcn_W"]
BIASES = ["uv_b1", "uv_b2", "uv_b3", "vu_b1", "vu_b2", "vu_b3"]

LAYER_2_AT, LAYER_3_AT, PROJECT_AT = 1, 3, 5
NORM_LAYER_2_AT, NORM_LAYER_3_AT, NORM_MEAN_AT, NORM_VAR_AT, NORM_PROJECT_AT = 0, 1, 3, 4, 6
LAST_MEAN_AT, LAST_VAR_AT = 0, 2


def gnn_kernel(nc, adj, x_t, weights, biases, out_t):
    with ExitStack() as ctx:
        def sbuf(name, shape, dtype=F32):
            return ctx.enter_context(nc.sbuf_tensor(name, shape, dtype))

        def psum(name, shape):
            return ctx.enter_context(nc.psum_tensor(name, shape, F32))

        def sem(name):
            return ctx.enter_context(nc.semaphore(name))

        raw = [sbuf(f"raw{s}", [D, GROUP]) for s in range(SLOTS)]
        high = [sbuf(f"high{s}", [D, GROUP], F32R) for s in range(SLOTS)]
        low = [sbuf(f"low{s}", [D, GROUP], F32R) for s in range(SLOTS)]
        p_high = [sbuf(f"p_high{i}", [D, N], F32R) for i in range(2)]
        p_low = [sbuf(f"p_low{i}", [D, N], F32R) for i in range(2)]
        resid = sbuf("resid", [D, N])
        w = {name: sbuf(f"w_{name}", [D, D]) for name in WEIGHTS}
        b = {name: sbuf(f"b_{name}", [D, 1]) for name in BIASES}
        average = sbuf("average", [D, D])
        eps = sbuf("eps", [D, 1])
        z = sbuf("z", [D, CHUNK])
        h = sbuf("h", [D, CHUNK])
        summed = sbuf("summed", [D, CHUNK])
        centered = sbuf("centered", [D, CHUNK])
        squared = sbuf("squared", [D, CHUNK])
        std = sbuf("std", [D, CHUNK])
        rstd = sbuf("rstd", [D, CHUNK])
        normed = [sbuf(f"normed{i}", [D, CHUNK]) for i in range(2)]

        acc = [psum(f"acc{i}", [D, CHUNK]) for i in range(2)]
        layer = psum("layer", [D, CHUNK])
        proj = [psum(f"proj{i}", [D, CHUNK]) for i in range(2)]
        mean = psum("mean", [D, CHUNK])
        var = psum("var", [D, CHUNK])

        x_loaded = sem("x_loaded")
        consts_loaded = sem("consts_loaded")
        consts_set = sem("consts_set")
        raw_loaded = [sem(f"raw_loaded{s}") for s in range(SLOTS)]
        high_ready = sem("high_ready")
        low_ready = sem("low_ready")
        group_used = sem("group_used")
        z_ready = sem("z_ready")
        h_ready = sem("h_ready")
        layer_done = sem("layer_done")
        proj_done = sem("proj_done")
        p_high_ready = sem("p_high_ready")
        p_low_ready = sem("p_low_ready")
        sum_ready = sem("sum_ready")
        mean_done = sem("mean_done")
        centered_ready = sem("centered_ready")
        squared_ready = sem("squared_ready")
        var_done = sem("var_done")
        std_ready = sem("std_ready")
        rstd_ready = sem("rstd_ready")
        normed_ready = sem("normed_ready")
        resid_ready = sem("resid_ready")
        out_stored = [sem(f"out_stored{i}") for i in range(2)]

        N_CONSTS = 16 * (len(WEIGHTS) - 1 + len(BIASES))

        def blocks_of(chunk):
            return bass.ds(chunk * CHUNK, CHUNK)

        block = ctx.enter_context(nc.Block())

        @block.sync
        def _(sp):
            sp.dma_start(w["uv_W1"][:], weights["uv_W1"]).then_inc(x_loaded, 16)
            sp.dma_start(resid[:], x_t).then_inc(x_loaded, 16)

            def load_step(step, chunk, peeled):
                for g in range(GROUPS):
                    if not peeled:
                        sp.wait_ge(low_ready, step * GROUPS + (g - SLOTS + 1))
                    elif g >= SLOTS:
                        sp.wait_ge(low_ready, g - SLOTS + 1)
                    sp.dma_start(raw[g % SLOTS][:], adj[chunk, g]).then_inc(raw_loaded[g % SLOTS], 16)

            load_step(0, 0, True)
            with sp.Fori(1, CHUNKS) as c:
                load_step(c, bass.ds(c, 1), False)
            with sp.Fori(1, PRODUCTS) as product:
                with sp.Fori(0, CHUNKS) as c:
                    load_step(product * CHUNKS + c, bass.ds(c, 1), False)

        @block.gpsimd
        def _(pool):
            nc.gpsimd.memset(average[:], 1.0 / D).then_inc(consts_set, 1)
            nc.gpsimd.memset(eps[:], EPS).then_inc(consts_set, 1)
            for name in WEIGHTS[1:]:
                pool.dma_start(w[name][:], weights[name]).then_inc(consts_loaded, 16)
            for name in BIASES:
                pool.dma_start(b[name][:], biases[name]).then_inc(consts_loaded, 16)
            with pool.Fori(0, CHUNKS - 1, 2) as c:
                for i in range(2):
                    pool.wait_ge(normed_ready, CHUNKS + c + i + 1)
                    pool.dma_start(out_t[bass.ds(c + i, 1)], normed[i][:]).then_inc(out_stored[i], 16)
            for i in range(2):
                pool.wait_ge(out_stored[i], 16 * CHUNKS // 2)

        @block.scalar
        def _(act):
            def split(group, slot, first=False):
                act.wait_ge(raw_loaded[slot], (group // SLOTS + 1) * 16 if first
                            else (group - slot) * (16 // SLOTS) + 16)
                if not (first and group < SLOTS):
                    act.wait_ge(group_used, group - SLOTS + 1)
                nc.scalar.activation(high[slot][:], raw[slot][:], ACT.Copy).then_inc(high_ready, 1)

            def biased(step, k, source, bias):
                ins = nc.scalar.activation(z[:], source[:], ACT.Identity, bias=bias[:])
                ins.then_inc(z_ready, 1)

            def project_high(step, chunk, side, parity):
                act.wait_ge(proj_done, CHUNKS + step + 1)
                nc.scalar.activation(p_high[parity][:, blocks_of(chunk)], proj[side][:],
                                     ACT.Copy).then_inc(p_high_ready, 1)

            def first_bias(step, side, way):
                act.wait_ge(group_used, (step + 1) * GROUPS)
                nc.scalar.activation(z[:], acc[side][:], ACT.Identity,
                                     bias=b[f"{way}_b1"][:]).then_inc(z_ready, 1)

            def later_bias(step, k, way):
                act.wait_ge(layer_done, step * 2 + k - 1)
                nc.scalar.activation(z[:], layer[:], ACT.Identity,
                                     bias=b[f"{way}_b{k}"][:]).then_inc(z_ready, 1)

            def squares(n):
                act.wait_ge(centered_ready, n + 1)
                nc.scalar.activation(squared[:], centered[:], ACT.Square).then_inc(squared_ready, 1)

            def deviation(n):
                act.wait_ge(var_done, n + 1)
                nc.scalar.activation(std[:], var[:], ACT.Sqrt, bias=eps[:]).then_inc(std_ready, 1)

            def keep_resid(n, chunk, side):
                act.wait_ge(normed_ready, n + 1)
                nc.scalar.activation(resid[:, blocks_of(chunk)], normed[side][:],
                                     ACT.Copy).then_inc(resid_ready, 1)

            def tail(step, chunk, side, stages, splits):
                for g in range(LEAD, LEAD + GROUPS):
                    for stage in stages.get(g - LEAD, ()):
                        stage()
                    if g < splits:
                        split((step + 1) * GROUPS + g, g % SLOTS)

            def round_tail(step, chunk, side, way, parity):
                tail(step, chunk, side, {
                    0: [lambda: first_bias(step, side, way)],
                    LAYER_2_AT + 1: [lambda: later_bias(step, 2, way)],
                    LAYER_3_AT + 1: [lambda: later_bias(step, 3, way)],
                    PROJECT_AT + 1: [lambda: project_high(step, chunk, side, parity)],
                }, LEAD + GROUPS)

            def norm_tail(step, chunk, side):
                n = step - NORM_STEP
                tail(step, chunk, side, {
                    0: [lambda: first_bias(step, side, "uv")],
                    NORM_LAYER_2_AT + 1: [lambda: later_bias(step, 2, "uv")],
                    NORM_LAYER_3_AT + 1: [lambda: later_bias(step, 3, "uv")],
                    NORM_MEAN_AT + 1: [lambda: squares(n)],
                    NORM_VAR_AT + 1: [lambda: deviation(n), lambda: keep_resid(n, chunk, side)],
                    NORM_PROJECT_AT + 1: [lambda: project_high(step, chunk, side, 1)],
                }, LEAD + GROUPS)

            def last_tail(step, chunk, side, splits):
                n = step - NORM_STEP
                tail(step, chunk, side, {
                    LAST_MEAN_AT + 1: [lambda: squares(n)],
                    LAST_VAR_AT + 1: [lambda: deviation(n)],
                }, splits)

            for c in range(CHUNKS):
                project_high(c - CHUNKS, c, c % 2, 0)
            for g in range(GROUPS + LEAD):
                split(g, g % SLOTS, True)
            act.wait_ge(consts_loaded, N_CONSTS)
            act.wait_ge(consts_set, 2)
            with act.Fori(0, ROUND_TRIPS) as trip:
                for i, way in enumerate(("uv", "vu")):
                    with act.Fori(0, CHUNKS - 1, 2) as c:
                        for side in range(2):
                            round_tail((trip * 2 + i) * CHUNKS + c + side, c + side, side, way, 1 - i)
            with act.Fori(0, CHUNKS - 1, 2) as c:
                for side in range(2):
                    norm_tail(NORM_STEP + c + side, c + side, side)
            with act.Fori(0, CHUNKS - 3, 2) as c:
                for side in range(2):
                    last_tail(LAST_STEP + c + side, c + side, side, LEAD + GROUPS)
            last_tail(STEPS - 2, CHUNKS - 2, 0, GROUPS)
            last_tail(STEPS - 1, CHUNKS - 1, 1, 0)

        @block.vector
        def _(dve):
            def split(group, slot, first=False):
                dve.wait_ge(high_ready, group + 1)
                if not (first and group < SLOTS):
                    dve.wait_ge(group_used, group - SLOTS + 1)
                nc.vector.tensor_tensor(low[slot][:], raw[slot][:], high[slot][:].bitcast(F32),
                                        ALU.subtract).then_inc(low_ready, 1)

            def leaky(step, k):
                dve.wait_ge(z_ready, step * 3 + k)
                nc.vector.scalar_tensor_tensor(out=h[:], in0=z[:], scalar=SLOPE, in1=z[:],
                                               op0=ALU.mult, op1=ALU.max).then_inc(h_ready, 1)

            def project_low(step, chunk, side, parity):
                dve.wait_ge(p_high_ready, CHUNKS + step + 1)
                nc.vector.tensor_tensor(p_low[parity][:, blocks_of(chunk)], proj[side][:],
                                        p_high[parity][:, blocks_of(chunk)].bitcast(F32),
                                        ALU.subtract).then_inc(p_low_ready, 1)

            def add_resid(step, chunk):
                dve.wait_ge(h_ready, step * 3 + 3)
                nc.vector.tensor_tensor(summed[:], h[:], resid[:, blocks_of(chunk)],
                                        ALU.add).then_inc(sum_ready, 1)

            def add_resid_last(step, chunk, side):
                dve.wait_ge(group_used, (step + 1) * GROUPS)
                nc.vector.tensor_tensor(summed[:], acc[side][:], resid[:, blocks_of(chunk)],
                                        ALU.add).then_inc(sum_ready, 1)

            def center(n):
                dve.wait_ge(mean_done, n + 1)
                nc.vector.tensor_tensor(centered[:], summed[:], mean[:],
                                        ALU.subtract).then_inc(centered_ready, 1)

            def norm(n, side, stored):
                dve.wait_ge(std_ready, n + 1)
                nc.vector.reciprocal(rstd[:], std[:]).then_inc(rstd_ready, 1)
                dve.wait_ge(rstd_ready, n + 1)
                if stored is not None:
                    dve.wait_ge(out_stored[side], stored)
                nc.vector.tensor_tensor(normed[side][:], centered[:], rstd[:],
                                        ALU.mult).then_inc(normed_ready, 1)

            def tail(step, stages, splits):
                for g in range(LEAD, LEAD + GROUPS):
                    for stage in stages.get(g - LEAD, ()):
                        stage()
                    if g < splits:
                        split((step + 1) * GROUPS + g, g % SLOTS)

            def round_tail(step, chunk, side, parity):
                tail(step, {
                    0: [lambda: leaky(step, 1)],
                    LAYER_2_AT + 1: [lambda: leaky(step, 2)],
                    LAYER_3_AT + 1: [lambda: leaky(step, 3)],
                    PROJECT_AT + 1: [lambda: project_low(step, chunk, side, parity)],
                }, LEAD + GROUPS)

            def norm_tail(step, chunk, side):
                n = step - NORM_STEP
                tail(step, {
                    0: [lambda: leaky(step, 1)],
                    NORM_LAYER_2_AT + 1: [lambda: leaky(step, 2)],
                    NORM_LAYER_3_AT + 1: [lambda: leaky(step, 3), lambda: add_resid(step, chunk)],
                    NORM_MEAN_AT + 1: [lambda: center(n)],
                    NORM_VAR_AT + 1: [lambda: norm(n, side, None)],
                    NORM_PROJECT_AT + 1: [lambda: project_low(step, chunk, side, 1)],
                }, LEAD + GROUPS)

            def last_tail(step, chunk, side, splits):
                n = step - NORM_STEP
                stored = (chunk - side) * 8 if not isinstance(chunk, int) or chunk >= 2 else None
                tail(step, {
                    0: [lambda: add_resid_last(step, chunk, side)],
                    LAST_MEAN_AT + 1: [lambda: center(n)],
                    LAST_VAR_AT + 1: [lambda: norm(n, side, stored)],
                }, splits)

            for c in range(CHUNKS):
                project_low(c - CHUNKS, c, c % 2, 0)
            for g in range(GROUPS + LEAD):
                split(g, g % SLOTS, True)
            with dve.Fori(0, ROUND_TRIPS) as trip:
                for i in range(2):
                    with dve.Fori(0, CHUNKS - 1, 2) as c:
                        for side in range(2):
                            round_tail((trip * 2 + i) * CHUNKS + c + side, c + side, side, 1 - i)
            with dve.Fori(0, CHUNKS - 1, 2) as c:
                for side in range(2):
                    norm_tail(NORM_STEP + c + side, c + side, side)
            dve.wait_ge(resid_ready, CHUNKS)
            for side in range(2):
                last_tail(LAST_STEP + side, side, side, LEAD + GROUPS)
            with dve.Fori(2, CHUNKS - 3, 2) as c:
                for side in range(2):
                    last_tail(LAST_STEP + c + side, c + side, side, LEAD + GROUPS)
            last_tail(STEPS - 2, CHUNKS - 2, 0, GROUPS)
            last_tail(STEPS - 1, CHUNKS - 1, 1, 0)

        @block.tensor
        def _(pe):
            def dense(weight, source, step, k):
                pe.wait_ge(h_ready, step * 3 + k - 1)
                nc.tensor.matmul(layer[:], weight[:], source[:], start=True,
                                 stop=True).then_inc(layer_done, 1)

            def project(step, weight, side, source):
                for j in range(CHUNK // D):
                    last = nc.tensor.matmul(proj[side][:, j * D:(j + 1) * D], source[:, j * D:(j + 1) * D],
                                            weight[:], start=True, stop=True)
                last.then_inc(proj_done, 1)

            def round_project(step, weight, side):
                pe.wait_ge(h_ready, step * 3 + 3)
                pe.wait_ge(p_low_ready, step + CHUNKS - 1)
                project(step, weight, side, h)

            def norm_project(step, side):
                pe.wait_ge(normed_ready, step - NORM_STEP + 1)
                pe.wait_ge(p_low_ready, step + CHUNKS - 1)
                project(step, w["gcn_W"], side, normed[side])

            def average_of(n, ready, source, target, done):
                pe.wait_ge(ready, n + 1)
                nc.tensor.matmul(target[:], average[:], source[:], start=True, stop=True).then_inc(done, 1)

            def round_stages(step, side, way, following):
                return {
                    LAYER_2_AT: lambda: dense(w[f"{way}_W2"], h, step, 2),
                    LAYER_3_AT: lambda: dense(w[f"{way}_W3"], h, step, 3),
                    PROJECT_AT: lambda: round_project(step, w[f"{following}_W1"], side),
                }

            def norm_stages(step, side):
                n = step - NORM_STEP
                return {
                    NORM_LAYER_2_AT: lambda: dense(w["uv_W2"], h, step, 2),
                    NORM_LAYER_3_AT: lambda: dense(w["uv_W3"], h, step, 3),
                    NORM_MEAN_AT: lambda: average_of(n, sum_ready, summed, mean, mean_done),
                    NORM_VAR_AT: lambda: average_of(n, squared_ready, squared, var, var_done),
                    NORM_PROJECT_AT: lambda: norm_project(step, side),
                }

            def last_stages(step):
                n = step - NORM_STEP
                return {
                    LAST_MEAN_AT: lambda: average_of(n, sum_ready, summed, mean, mean_done),
                    LAST_VAR_AT: lambda: average_of(n, squared_ready, squared, var, var_done),
                }

            def multiply(step, side, parity, stages, opens=False):
                for g in range(GROUPS):
                    slot = g % SLOTS
                    if opens:
                        pe.wait_ge(p_low_ready, step + g + 1)
                    pe.wait_ge(high_ready, step * GROUPS + g + 1)
                    for j in range(PER_GROUP):
                        at = (g * PER_GROUP + j) * D
                        for part in (p_high, p_low):
                            nc.tensor.matmul(acc[side][:], part[parity][:, at:at + D],
                                             high[slot][:, j * CHUNK:(j + 1) * CHUNK],
                                             start=(g == 0 and j == 0 and part is p_high), stop=False)
                    pe.wait_ge(low_ready, step * GROUPS + g + 1)
                    for j in range(PER_GROUP):
                        at = (g * PER_GROUP + j) * D
                        last = nc.tensor.matmul(acc[side][:], p_high[parity][:, at:at + D],
                                                low[slot][:, j * CHUNK:(j + 1) * CHUNK],
                                                start=False, stop=(g == GROUPS - 1 and j == PER_GROUP - 1))
                    last.then_inc(group_used, 1)
                    if g in stages:
                        stages[g]()

            pe.wait_ge(x_loaded, 32)
            for c in range(CHUNKS):
                if c >= 2:
                    pe.wait_ge(p_low_ready, c - 1)
                project(c - CHUNKS, w["uv_W1"], c % 2, resid[:, c * CHUNK:(c + 1) * CHUNK])
            multiply(0, 0, 0, {}, opens=True)
            pe.wait_ge(consts_loaded, N_CONSTS)
            pe.wait_ge(consts_set, 2)

            def product(start, parity, tails, ending):
                with pe.Fori(1, CHUNKS - 2, 2) as c:
                    for i in range(2):
                        multiply(start + c + i, (1 + i) % 2, parity, tails(start + c + i - 1, i % 2))
                multiply(start + CHUNKS - 1, 1, parity, tails(start + CHUNKS - 2, 0))
                if ending:
                    multiply(start + CHUNKS, 0, 1 - parity, tails(start + CHUNKS - 1, 1), opens=True)

            with pe.Fori(0, ROUND_TRIPS) as trip:
                for i, (way, following) in enumerate((("uv", "vu"), ("vu", "uv"))):
                    product((trip * 2 + i) * CHUNKS, i,
                            lambda step, side: round_stages(step, side, way, following), True)
            product(NORM_STEP, 0, norm_stages, True)
            product(LAST_STEP, 1, lambda step, side: last_stages(step), False)
            for stage in last_stages(STEPS - 1).values():
                stage()


_WEIGHTS = {"uv_W1": "L0_gnn_uv_W1", "uv_W2": "L0_gnn_uv_W2", "uv_W3": "L0_gnn_uv_W3",
            "vu_W1": "L0_gnn_vu_W1", "vu_W2": "L0_gnn_vu_W2", "vu_W3": "L0_gnn_vu_W3",
            "gcn_W": "L1_gnn_weight"}
_BIASES = {"uv_b1": "L0_gnn_uv_b1", "uv_b2": "L0_gnn_uv_b2", "uv_b3": "L0_gnn_uv_b3",
           "vu_b1": "L0_gnn_vu_b1", "vu_b2": "L0_gnn_vu_b2", "vu_b3": "L0_gnn_vu_b3"}


def kernel(**inputs):
    import numpy as _np
    import concourse.bacc as _bacc
    from concourse.bass_utils import run_bass_kernel_spmd as _run

    nc = _bacc.Bacc("TRN2", target_bir_lowering=False, num_devices=1)
    arrays = {}

    def put(name, array):
        arrays[name] = _np.ascontiguousarray(array)
        return nc.dram_tensor(name, arrays[name].shape, F32, kind="ExternalInput").ap()

    adj = _np.asarray(inputs["adj"]).reshape(CHUNKS, CHUNK, GROUPS, PER_GROUP, D)
    adj = put("adj_dram", adj.transpose(0, 2, 4, 3, 1).reshape(CHUNKS, GROUPS, D, GROUP))
    x_t = put("x_t_dram", _np.asarray(inputs["x"]).T)
    weights = {k: put(f"{k}_dram", inputs[v]) for k, v in _WEIGHTS.items()}
    biases = {k: put(f"{k}_dram", _np.asarray(inputs[v]).reshape(D, 1)) for k, v in _BIASES.items()}
    out_t = nc.dram_tensor("out_t_dram", (CHUNKS, D, CHUNK), F32, kind="ExternalOutput").ap()
    gnn_kernel(nc, adj, x_t, weights, biases, out_t)
    r = _run(nc, [arrays], core_ids=[0])
    got = r.results[0]["out_t_dram"]
    return _np.ascontiguousarray(got.transpose(0, 2, 1).reshape(N, D))
```

```python
from contextlib import ExitStack

import concourse.bass as bass
from concourse import mybir

F32 = mybir.dt.float32
F32R = mybir.dt.float32r
ALU = mybir.AluOpType
ACT = mybir.ActivationFunctionType

N = 4096
D = 128
CHUNK = 512
CHUNKS = N // CHUNK
BLOCKS = N // D
GROUPS = 8
PER_GROUP = BLOCKS // GROUPS
GROUP = PER_GROUP * CHUNK
SLOTS = 4
LEAD = SLOTS - 1
ROUND_TRIPS = 2
PRODUCTS = 2 * ROUND_TRIPS + 2
STEPS = PRODUCTS * CHUNKS
NORM_STEP = (PRODUCTS - 2) * CHUNKS
LAST_STEP = (PRODUCTS - 1) * CHUNKS
SLOPE = 0.01
EPS = 1e-5

WEIGHTS = ["uv_W1", "uv_W2", "uv_W3", "vu_W1", "vu_W2", "vu_W3", "gcn_W"]
BIASES = ["uv_b1", "uv_b2", "uv_b3", "vu_b1", "vu_b2", "vu_b3"]

LAYER_2_AT, LAYER_3_AT, PROJECT_AT = 1, 3, 5
NORM_LAYER_2_AT, NORM_LAYER_3_AT, NORM_CENTER_AT, NORM_VAR_AT, NORM_PROJECT_AT, NORM_SPREAD_AT = 0, 1, 3, 4, 5, 6
LAST_CENTER_AT, LAST_VAR_AT, LAST_SPREAD_AT = 1, 2, 5


def gnn_kernel(nc, adj, x_t, weights, biases, out_t):
    with ExitStack() as ctx:
        def sbuf(name, shape, dtype=F32):
            return ctx.enter_context(nc.sbuf_tensor(name, shape, dtype))

        def psum(name, shape):
            return ctx.enter_context(nc.psum_tensor(name, shape, F32))

        def sem(name):
            return ctx.enter_context(nc.semaphore(name))

        raw = [sbuf(f"raw{s}", [D, GROUP]) for s in range(SLOTS)]
        high = [sbuf(f"high{s}", [D, GROUP], F32R) for s in range(SLOTS)]
        low = [sbuf(f"low{s}", [D, GROUP], F32R) for s in range(SLOTS)]
        p_high = [sbuf(f"p_high{i}", [D, N], F32R) for i in range(2)]
        p_low = [sbuf(f"p_low{i}", [D, N], F32R) for i in range(2)]
        resid = sbuf("resid", [D, N])
        w = {name: sbuf(f"w_{name}", [D, D]) for name in WEIGHTS}
        b = {name: sbuf(f"b_{name}", [D, 1]) for name in BIASES}
        average = sbuf("average", [D, 1])
        centering = sbuf("centering", [D, D])
        identity = sbuf("identity", [D, D])
        ones = sbuf("ones", [D, D])
        eps = sbuf("eps", [D, 1])
        z = sbuf("z", [D, CHUNK])
        h = sbuf("h", [D, CHUNK])
        summed = sbuf("summed", [D, CHUNK])
        centered = sbuf("centered", [D, CHUNK])
        squared = sbuf("squared", [D, CHUNK])
        std = sbuf("std", [D, CHUNK // D])
        rstd = sbuf("rstd", [D, CHUNK // D])
        diagonal = sbuf("diagonal", [D, CHUNK])
        normed = [sbuf(f"normed{i}", [D, CHUNK]) for i in range(2)]

        acc = [psum(f"acc{i}", [D, CHUNK]) for i in range(2)]
        layer = psum("layer", [D, CHUNK])
        proj = [psum(f"proj{i}", [D, CHUNK]) for i in range(2)]
        minus_mean = psum("minus_mean", [D, CHUNK])
        var = psum("var", [D, CHUNK])
        spread = psum("spread", [D, CHUNK])

        x_loaded = sem("x_loaded")
        consts_loaded = sem("consts_loaded")
        consts_set = sem("consts_set")
        raw_loaded = [sem(f"raw_loaded{s}") for s in range(SLOTS)]
        high_ready = sem("high_ready")
        low_ready = sem("low_ready")
        group_used = sem("group_used")
        z_ready = sem("z_ready")
        h_ready = sem("h_ready")
        layer_done = sem("layer_done")
        proj_done = sem("proj_done")
        p_high_ready = sem("p_high_ready")
        p_low_ready = sem("p_low_ready")
        sum_ready = sem("sum_ready")
        center_done = sem("center_done")
        centered_ready = sem("centered_ready")
        squared_ready = sem("squared_ready")
        var_done = sem("var_done")
        std_ready = sem("std_ready")
        rstd_ready = sem("rstd_ready")
        diagonal_ready = sem("diagonal_ready")
        spread_done = sem("spread_done")
        normed_ready = sem("normed_ready")
        out_stored = [sem(f"out_stored{i}") for i in range(2)]

        CONSTS_SET = 7
        N_CONSTS = 16 * (len(WEIGHTS) - 1 + len(BIASES))

        IN_CHUNK = CHUNK // D

        def blocks_of(chunk):
            return bass.ds(chunk * CHUNK, CHUNK)

        def block_of(chunk, j):
            return bass.ds(chunk * CHUNK + j * D, D)

        def block_in(tile, j):
            return tile[:, j * D:(j + 1) * D]

        block = ctx.enter_context(nc.Block())

        @block.sync
        def _(sp):
            sp.dma_start(w["uv_W1"][:], weights["uv_W1"]).then_inc(x_loaded, 16)
            sp.dma_start(resid[:], x_t).then_inc(x_loaded, 16)

            def load_step(step, chunk, peeled):
                for g in range(GROUPS):
                    if not peeled:
                        sp.wait_ge(low_ready, step * GROUPS + (g - SLOTS + 1))
                    elif g >= SLOTS:
                        sp.wait_ge(low_ready, g - SLOTS + 1)
                    sp.dma_start(raw[g % SLOTS][:], adj[chunk, g]).then_inc(raw_loaded[g % SLOTS], 16)

            load_step(0, 0, True)
            with sp.Fori(1, CHUNKS) as c:
                load_step(c, bass.ds(c, 1), False)
            with sp.Fori(1, PRODUCTS) as product:
                with sp.Fori(0, CHUNKS) as c:
                    load_step(product * CHUNKS + c, bass.ds(c, 1), False)

        @block.gpsimd
        def _(pool):
            nc.gpsimd.memset(average[:], 1.0 / D).then_inc(consts_set, 1)
            nc.gpsimd.memset(eps[:], EPS).then_inc(consts_set, 1)
            nc.gpsimd.memset(ones[:], 1.0).then_inc(consts_set, 1)
            nc.gpsimd.memset(identity[:], 0.0).then_inc(consts_set, 1)
            nc.gpsimd.memset(centering[:], -1.0 / D).then_inc(consts_set, 1)
            pool.wait_ge(consts_set, 5)
            for matrix, diagonal_value in ((identity, 1.0), (centering, 1.0 - 1.0 / D)):
                nc.gpsimd.affine_select(out=matrix[:], in_=matrix[:], compare_op=ALU.not_equal,
                                        fill=diagonal_value, base=0, pattern=[[-1, D]],
                                        channel_multiplier=1).then_inc(consts_set, 1)
            for name in WEIGHTS[1:]:
                pool.dma_start(w[name][:], weights[name]).then_inc(consts_loaded, 16)
            for name in BIASES:
                pool.dma_start(b[name][:], biases[name]).then_inc(consts_loaded, 16)
            with pool.Fori(0, CHUNKS - 1, 2) as c:
                for i in range(2):
                    pool.wait_ge(normed_ready, CHUNKS + c + i + 1)
                    pool.dma_start(out_t[bass.ds(c + i, 1)], normed[i][:]).then_inc(out_stored[i], 16)
            for i in range(2):
                pool.wait_ge(out_stored[i], 16 * CHUNKS // 2)

        @block.scalar
        def _(act):
            def split(group, slot, first=False):
                act.wait_ge(raw_loaded[slot], (group // SLOTS + 1) * 16 if first
                            else (group - slot) * (16 // SLOTS) + 16)
                if not (first and group < SLOTS):
                    act.wait_ge(group_used, group - SLOTS + 1)
                nc.scalar.activation(high[slot][:], raw[slot][:], ACT.Copy).then_inc(high_ready, 1)

            def project_high(step, chunk, side, parity):
                act.wait_ge(proj_done, CHUNKS + step + 1)
                nc.scalar.activation(p_high[parity][:, blocks_of(chunk)], proj[side][:],
                                     ACT.Copy).then_inc(p_high_ready, 1)

            def first_bias(step, side, way):
                act.wait_ge(group_used, (step + 1) * GROUPS)
                nc.scalar.activation(z[:], acc[side][:], ACT.Identity,
                                     bias=b[f"{way}_b1"][:]).then_inc(z_ready, 1)

            def later_bias(step, k, way):
                act.wait_ge(layer_done, step * 2 + k - 1)
                nc.scalar.activation(z[:], layer[:], ACT.Identity,
                                     bias=b[f"{way}_b{k}"][:]).then_inc(z_ready, 1)

            def squares(n):
                act.wait_ge(center_done, n + 1)
                nc.scalar.activation(squared[:], minus_mean[:], ACT.Square).then_inc(squared_ready, 1)
                nc.scalar.activation(centered[:], minus_mean[:], ACT.Copy).then_inc(centered_ready, 1)

            def deviation(n):
                act.wait_ge(var_done, n + 1)
                nc.scalar.activation(std[:], var[:, 0:IN_CHUNK], ACT.Sqrt, bias=eps[:]).then_inc(std_ready, 1)

            def diagonals(n):
                act.wait_ge(rstd_ready, n + 1)
                for j in range(IN_CHUNK):
                    last = nc.scalar.activation(block_in(diagonal, j), identity[:], ACT.Copy,
                                                scale=rstd[:, j:j + 1])
                last.then_inc(diagonal_ready, 1)

            def project_norm_high(step, chunk, side):
                act.wait_ge(rstd_ready, step - NORM_STEP + 1)
                act.wait_ge(proj_done, CHUNKS + step + 1)
                for j in range(IN_CHUNK):
                    last = nc.scalar.activation(p_high[1][:, block_of(chunk, j)], block_in(proj[side], j),
                                                ACT.Copy, scale=rstd[:, j:j + 1])
                last.then_inc(p_high_ready, 1)

            def tail(step, chunk, side, stages, splits):
                for g in range(LEAD, LEAD + GROUPS):
                    for stage in stages.get(g - LEAD, ()):
                        stage()
                    if g < splits:
                        split((step + 1) * GROUPS + g, g % SLOTS)

            def round_tail(step, chunk, side, way, parity):
                tail(step, chunk, side, {
                    0: [lambda: first_bias(step, side, way)],
                    LAYER_2_AT + 1: [lambda: later_bias(step, 2, way)],
                    LAYER_3_AT + 1: [lambda: later_bias(step, 3, way)],
                    PROJECT_AT + 1: [lambda: project_high(step, chunk, side, parity)],
                }, LEAD + GROUPS)

            def norm_tail(step, chunk, side):
                n = step - NORM_STEP
                tail(step, chunk, side, {
                    0: [lambda: first_bias(step, side, "uv")],
                    NORM_LAYER_2_AT + 1: [lambda: later_bias(step, 2, "uv")],
                    NORM_LAYER_3_AT + 1: [lambda: later_bias(step, 3, "uv")],
                    NORM_CENTER_AT + 1: [lambda: squares(n)],
                    NORM_VAR_AT + 1: [lambda: deviation(n)],
                    NORM_PROJECT_AT + 1: [lambda: diagonals(n),
                                          lambda: project_norm_high(step, chunk, side)],
                }, LEAD + GROUPS)

            def last_tail(step, chunk, side, splits):
                n = step - NORM_STEP
                tail(step, chunk, side, {
                    LAST_CENTER_AT + 1: [lambda: squares(n)],
                    LAST_VAR_AT + 1: [lambda: deviation(n)],
                    LAST_SPREAD_AT: [lambda: diagonals(n)],
                }, splits)

            for c in range(CHUNKS):
                project_high(c - CHUNKS, c, c % 2, 0)
            for g in range(GROUPS + LEAD):
                split(g, g % SLOTS, True)
            act.wait_ge(consts_loaded, N_CONSTS)
            act.wait_ge(consts_set, CONSTS_SET)
            with act.Fori(0, ROUND_TRIPS) as trip:
                for i, way in enumerate(("uv", "vu")):
                    with act.Fori(0, CHUNKS - 1, 2) as c:
                        for side in range(2):
                            round_tail((trip * 2 + i) * CHUNKS + c + side, c + side, side, way, 1 - i)
            with act.Fori(0, CHUNKS - 1, 2) as c:
                for side in range(2):
                    norm_tail(NORM_STEP + c + side, c + side, side)
            with act.Fori(0, CHUNKS - 3, 2) as c:
                for side in range(2):
                    last_tail(LAST_STEP + c + side, c + side, side, LEAD + GROUPS)
            last_tail(STEPS - 2, CHUNKS - 2, 0, GROUPS)
            last_tail(STEPS - 1, CHUNKS - 1, 1, 0)

        @block.vector
        def _(dve):
            def split(group, slot, first=False):
                dve.wait_ge(high_ready, group + 1)
                if not (first and group < SLOTS):
                    dve.wait_ge(group_used, group - SLOTS + 1)
                nc.vector.tensor_tensor(low[slot][:], raw[slot][:], high[slot][:].bitcast(F32),
                                        ALU.subtract).then_inc(low_ready, 1)

            def leaky(step, k):
                dve.wait_ge(z_ready, step * 3 + k)
                nc.vector.scalar_tensor_tensor(out=h[:], in0=z[:], scalar=SLOPE, in1=z[:],
                                               op0=ALU.mult, op1=ALU.max).then_inc(h_ready, 1)

            def project_low(step, chunk, side, parity):
                dve.wait_ge(p_high_ready, CHUNKS + step + 1)
                nc.vector.tensor_tensor(p_low[parity][:, blocks_of(chunk)], proj[side][:],
                                        p_high[parity][:, blocks_of(chunk)].bitcast(F32),
                                        ALU.subtract).then_inc(p_low_ready, 1)

            def add_resid(step, chunk):
                dve.wait_ge(h_ready, step * 3 + 3)
                nc.vector.tensor_tensor(summed[:], h[:], resid[:, blocks_of(chunk)],
                                        ALU.add).then_inc(sum_ready, 1)

            def add_resid_last(step, chunk, side):
                dve.wait_ge(group_used, (step + 1) * GROUPS)
                nc.vector.tensor_tensor(summed[:], acc[side][:], resid[:, blocks_of(chunk)],
                                        ALU.add).then_inc(sum_ready, 1)

            def invert(n):
                dve.wait_ge(std_ready, n + 1)
                nc.vector.reciprocal(rstd[:], std[:]).then_inc(rstd_ready, 1)

            def project_norm_low(step, chunk, side):
                dve.wait_ge(rstd_ready, step - NORM_STEP + 1)
                dve.wait_ge(p_high_ready, CHUNKS + step + 1)
                for j in range(IN_CHUNK):
                    last = nc.vector.scalar_tensor_tensor(
                        out=p_low[1][:, block_of(chunk, j)], in0=block_in(proj[side], j),
                        scalar=rstd[:, j:j + 1], in1=p_high[1][:, block_of(chunk, j)].bitcast(F32),
                        op0=ALU.mult, op1=ALU.subtract)
                last.then_inc(p_low_ready, 1)

            def norm(n, target):
                dve.wait_ge(spread_done, n + 1)
                dve.wait_ge(centered_ready, n + 1)
                nc.vector.tensor_tensor(target, centered[:], spread[:], ALU.mult).then_inc(normed_ready, 1)

            def norm_out(n, side, stored):
                if stored is not None:
                    dve.wait_ge(out_stored[side], stored)
                norm(n, normed[side][:])

            def tail(step, stages, splits):
                for g in range(LEAD, LEAD + GROUPS):
                    for stage in stages.get(g - LEAD, ()):
                        stage()
                    if g < splits:
                        split((step + 1) * GROUPS + g, g % SLOTS)

            def round_tail(step, chunk, side, parity):
                tail(step, {
                    0: [lambda: leaky(step, 1)],
                    LAYER_2_AT + 1: [lambda: leaky(step, 2)],
                    LAYER_3_AT + 1: [lambda: leaky(step, 3)],
                    PROJECT_AT + 1: [lambda: project_low(step, chunk, side, parity)],
                }, LEAD + GROUPS)

            def norm_tail(step, chunk, side):
                n = step - NORM_STEP
                tail(step, {
                    0: [lambda: leaky(step, 1)],
                    NORM_LAYER_2_AT + 1: [lambda: leaky(step, 2)],
                    NORM_LAYER_3_AT + 1: [lambda: leaky(step, 3), lambda: add_resid(step, chunk)],
                    NORM_VAR_AT + 1: [lambda: invert(n)],
                    NORM_PROJECT_AT + 1: [lambda: project_norm_low(step, chunk, side)],
                    NORM_SPREAD_AT + 1: [lambda: norm(n, resid[:, blocks_of(chunk)])],
                }, LEAD + GROUPS)

            def last_tail(step, chunk, side, splits):
                n = step - NORM_STEP
                stored = (chunk - side) * 8 if not isinstance(chunk, int) or chunk >= 2 else None
                tail(step, {
                    0: [lambda: add_resid_last(step, chunk, side)],
                    LAST_VAR_AT + 1: [lambda: invert(n)],
                    LAST_SPREAD_AT + 1: [lambda: norm_out(n, side, stored)],
                }, splits)

            for c in range(CHUNKS):
                project_low(c - CHUNKS, c, c % 2, 0)
            for g in range(GROUPS + LEAD):
                split(g, g % SLOTS, True)
            with dve.Fori(0, ROUND_TRIPS) as trip:
                for i in range(2):
                    with dve.Fori(0, CHUNKS - 1, 2) as c:
                        for side in range(2):
                            round_tail((trip * 2 + i) * CHUNKS + c + side, c + side, side, 1 - i)
            with dve.Fori(0, CHUNKS - 1, 2) as c:
                for side in range(2):
                    norm_tail(NORM_STEP + c + side, c + side, side)
            dve.wait_ge(normed_ready, CHUNKS)
            for side in range(2):
                last_tail(LAST_STEP + side, side, side, LEAD + GROUPS)
            with dve.Fori(2, CHUNKS - 3, 2) as c:
                for side in range(2):
                    last_tail(LAST_STEP + c + side, c + side, side, LEAD + GROUPS)
            last_tail(STEPS - 2, CHUNKS - 2, 0, GROUPS)
            last_tail(STEPS - 1, CHUNKS - 1, 1, 0)

        @block.tensor
        def _(pe):
            def dense(weight, source, step, k):
                pe.wait_ge(h_ready, step * 3 + k - 1)
                nc.tensor.matmul(layer[:], weight[:], source[:], start=True,
                                 stop=True).then_inc(layer_done, 1)

            def project(step, weight, side, source):
                for j in range(CHUNK // D):
                    last = nc.tensor.matmul(proj[side][:, j * D:(j + 1) * D], source[:, j * D:(j + 1) * D],
                                            weight[:], start=True, stop=True)
                last.then_inc(proj_done, 1)

            def round_project(step, weight, side):
                pe.wait_ge(h_ready, step * 3 + 3)
                pe.wait_ge(p_low_ready, step + CHUNKS - 1)
                project(step, weight, side, h)

            def center(n):
                pe.wait_ge(sum_ready, n + 1)
                nc.tensor.matmul(minus_mean[:], centering[:], summed[:], start=True,
                                 stop=True).then_inc(center_done, 1)

            def variance(n):
                pe.wait_ge(squared_ready, n + 1)
                for j in range(IN_CHUNK):
                    last = nc.tensor.matmul(var[:, j:j + 1], block_in(squared, j), average[:],
                                            start=True, stop=True)
                last.then_inc(var_done, 1)

            def norm_project(step, side):
                pe.wait_ge(centered_ready, step - NORM_STEP + 1)
                pe.wait_ge(p_low_ready, step + CHUNKS - 1)
                project(step, w["gcn_W"], side, centered)

            def spread_deviation(n):
                pe.wait_ge(diagonal_ready, n + 1)
                nc.tensor.matmul(spread[:], ones[:], diagonal[:], start=True,
                                 stop=True).then_inc(spread_done, 1)

            def round_stages(step, side, way, following):
                return {
                    LAYER_2_AT: lambda: dense(w[f"{way}_W2"], h, step, 2),
                    LAYER_3_AT: lambda: dense(w[f"{way}_W3"], h, step, 3),
                    PROJECT_AT: lambda: round_project(step, w[f"{following}_W1"], side),
                }

            def norm_stages(step, side):
                n = step - NORM_STEP
                return {
                    NORM_LAYER_2_AT: lambda: dense(w["uv_W2"], h, step, 2),
                    NORM_LAYER_3_AT: lambda: dense(w["uv_W3"], h, step, 3),
                    NORM_CENTER_AT: lambda: center(n),
                    NORM_VAR_AT: lambda: variance(n),
                    NORM_PROJECT_AT: lambda: norm_project(step, side),
                    NORM_SPREAD_AT: lambda: spread_deviation(n),
                }

            def last_stages(step):
                n = step - NORM_STEP
                return {
                    LAST_CENTER_AT: lambda: center(n),
                    LAST_VAR_AT: lambda: variance(n),
                    LAST_SPREAD_AT: lambda: spread_deviation(n),
                }

            def multiply(step, side, parity, stages, opens=False):
                for g in range(GROUPS):
                    slot = g % SLOTS
                    if opens:
                        pe.wait_ge(p_low_ready, step + g + 1)
                    pe.wait_ge(high_ready, step * GROUPS + g + 1)
                    for j in range(PER_GROUP):
                        at = (g * PER_GROUP + j) * D
                        for part in (p_high, p_low):
                            nc.tensor.matmul(acc[side][:], part[parity][:, at:at + D],
                                             high[slot][:, j * CHUNK:(j + 1) * CHUNK],
                                             start=(g == 0 and j == 0 and part is p_high), stop=False)
                    pe.wait_ge(low_ready, step * GROUPS + g + 1)
                    for j in range(PER_GROUP):
                        at = (g * PER_GROUP + j) * D
                        last = nc.tensor.matmul(acc[side][:], p_high[parity][:, at:at + D],
                                                low[slot][:, j * CHUNK:(j + 1) * CHUNK],
                                                start=False, stop=(g == GROUPS - 1 and j == PER_GROUP - 1))
                    last.then_inc(group_used, 1)
                    if g in stages:
                        stages[g]()

            pe.wait_ge(x_loaded, 32)
            for c in range(CHUNKS):
                if c >= 2:
                    pe.wait_ge(p_low_ready, c - 1)
                project(c - CHUNKS, w["uv_W1"], c % 2, resid[:, c * CHUNK:(c + 1) * CHUNK])
            multiply(0, 0, 0, {}, opens=True)
            pe.wait_ge(consts_loaded, N_CONSTS)
            pe.wait_ge(consts_set, CONSTS_SET)

            def product(start, parity, tails, ending):
                with pe.Fori(1, CHUNKS - 2, 2) as c:
                    for i in range(2):
                        multiply(start + c + i, (1 + i) % 2, parity, tails(start + c + i - 1, i % 2))
                multiply(start + CHUNKS - 1, 1, parity, tails(start + CHUNKS - 2, 0))
                if ending:
                    multiply(start + CHUNKS, 0, 1 - parity, tails(start + CHUNKS - 1, 1), opens=True)

            with pe.Fori(0, ROUND_TRIPS) as trip:
                for i, (way, following) in enumerate((("uv", "vu"), ("vu", "uv"))):
                    product((trip * 2 + i) * CHUNKS, i,
                            lambda step, side: round_stages(step, side, way, following), True)
            product(NORM_STEP, 0, norm_stages, True)
            product(LAST_STEP, 1, lambda step, side: last_stages(step), False)
            for stage in last_stages(STEPS - 1).values():
                stage()


_WEIGHTS = {"uv_W1": "L0_gnn_uv_W1", "uv_W2": "L0_gnn_uv_W2", "uv_W3": "L0_gnn_uv_W3",
            "vu_W1": "L0_gnn_vu_W1", "vu_W2": "L0_gnn_vu_W2", "vu_W3": "L0_gnn_vu_W3",
            "gcn_W": "L1_gnn_weight"}
_BIASES = {"uv_b1": "L0_gnn_uv_b1", "uv_b2": "L0_gnn_uv_b2", "uv_b3": "L0_gnn_uv_b3",
           "vu_b1": "L0_gnn_vu_b1", "vu_b2": "L0_gnn_vu_b2", "vu_b3": "L0_gnn_vu_b3"}


def kernel(**inputs):
    import numpy as _np
    import concourse.bacc as _bacc
    from concourse.bass_utils import run_bass_kernel_spmd as _run

    nc = _bacc.Bacc("TRN2", target_bir_lowering=False, num_devices=1)
    arrays = {}

    def put(name, array):
        arrays[name] = _np.ascontiguousarray(array)
        return nc.dram_tensor(name, arrays[name].shape, F32, kind="ExternalInput").ap()

    adj = _np.asarray(inputs["adj"]).reshape(CHUNKS, CHUNK, GROUPS, PER_GROUP, D)
    adj = put("adj_dram", adj.transpose(0, 2, 4, 3, 1).reshape(CHUNKS, GROUPS, D, GROUP))
    x_t = put("x_t_dram", _np.asarray(inputs["x"]).T)
    weights = {k: put(f"{k}_dram", inputs[v]) for k, v in _WEIGHTS.items()}
    biases = {k: put(f"{k}_dram", _np.asarray(inputs[v]).reshape(D, 1)) for k, v in _BIASES.items()}
    out_t = nc.dram_tensor("out_t_dram", (CHUNKS, D, CHUNK), F32, kind="ExternalOutput").ap()
    gnn_kernel(nc, adj, x_t, weights, biases, out_t)
    r = _run(nc, [arrays], core_ids=[0])
    got = r.results[0]["out_t_dram"]
    return _np.ascontiguousarray(got.transpose(0, 2, 1).reshape(N, D))
```

```python
from contextlib import ExitStack

import concourse.bass as bass
from concourse import mybir

F32 = mybir.dt.float32
F32R = mybir.dt.float32r
ALU = mybir.AluOpType
ACT = mybir.ActivationFunctionType

N = 4096
D = 128
CHUNK = 512
CHUNKS = N // CHUNK
BLOCKS = N // D
GROUPS = 8
PER_GROUP = BLOCKS // GROUPS
GROUP = PER_GROUP * CHUNK
SLOTS = 4
LEAD = SLOTS - 1
KEPT = 2
ROUND_TRIPS = 2
PRODUCTS = 2 * ROUND_TRIPS + 2
STEPS = PRODUCTS * CHUNKS
NORM_STEP = (PRODUCTS - 2) * CHUNKS
LAST_STEP = (PRODUCTS - 1) * CHUNKS
SLOPE = 0.01
EPS = 1e-5

WEIGHTS = ["uv_W1", "uv_W2", "uv_W3", "vu_W1", "vu_W2", "vu_W3", "gcn_W"]
BIASES = ["uv_b1", "uv_b2", "uv_b3", "vu_b1", "vu_b2", "vu_b3"]

LAYER_2_AT, LAYER_3_AT, PROJECT_AT = 1, 3, 5
NORM_LAYER_2_AT, NORM_LAYER_3_AT, NORM_CENTER_AT, NORM_VAR_AT, NORM_PROJECT_AT, NORM_SPREAD_AT = 1, 2, 4, 5, 6, 6
LAST_CENTER_AT, LAST_VAR_AT, LAST_SPREAD_AT = 1, 2, 5


def gnn_kernel(nc, adj, x_t, weights, biases, out_t):
    with ExitStack() as ctx:
        def sbuf(name, shape, dtype=F32):
            return ctx.enter_context(nc.sbuf_tensor(name, shape, dtype))

        def psum(name, shape):
            return ctx.enter_context(nc.psum_tensor(name, shape, F32))

        def sem(name):
            return ctx.enter_context(nc.semaphore(name))

        raw = [sbuf(f"raw{s}", [D, GROUP]) for s in range(SLOTS)]
        kept = [sbuf(f"kept{k}", [D, GROUP]) for k in range(KEPT)]
        high = [sbuf(f"high{s}", [D, GROUP], F32R) for s in range(SLOTS)]
        low = [sbuf(f"low{s}", [D, GROUP], F32R) for s in range(SLOTS)]
        p_high = [sbuf(f"p_high{i}", [D, N], F32R) for i in range(2)]
        p_low = [sbuf(f"p_low{i}", [D, N], F32R) for i in range(2)]
        resid = sbuf("resid", [D, N])
        w = {name: sbuf(f"w_{name}", [D, D]) for name in WEIGHTS}
        b = {name: sbuf(f"b_{name}", [D, 1]) for name in BIASES}
        average = sbuf("average", [D, 1])
        centering = sbuf("centering", [D, D])
        identity = sbuf("identity", [D, D])
        ones = sbuf("ones", [D, D])
        eps = sbuf("eps", [D, 1])
        z = sbuf("z", [D, CHUNK])
        h = sbuf("h", [D, CHUNK])
        centered = sbuf("centered", [D, CHUNK])
        squared = sbuf("squared", [D, CHUNK])
        repeated = squared
        std = sbuf("std", [D, CHUNK // D])
        rstd = sbuf("rstd", [D, CHUNK // D])
        normed = [z, sbuf("normed1", [D, CHUNK])]

        acc = [psum(f"acc{i}", [D, CHUNK]) for i in range(2)]
        layer = psum("layer", [D, CHUNK])
        proj = [psum(f"proj{i}", [D, CHUNK]) for i in range(2)]
        minus_mean = psum("minus_mean", [D, CHUNK])
        var = psum("var", [D, CHUNK])
        spread = psum("spread", [D, CHUNK])

        x_loaded = [sem("x_loaded_first"), sem("x_loaded_rest")]
        kept_loaded = [sem(f"kept_loaded{k}") for k in range(KEPT)]
        consts_loaded = sem("consts_loaded")
        consts_set = sem("consts_set")
        raw_loaded = [sem(f"raw_loaded{s}") for s in range(SLOTS)]
        high_ready = sem("high_ready")
        low_ready = sem("low_ready")
        group_used = sem("group_used")
        z_ready = sem("z_ready")
        h_ready = sem("h_ready")
        layer_done = sem("layer_done")
        proj_done = sem("proj_done")
        p_high_ready = sem("p_high_ready")
        p_low_ready = sem("p_low_ready")
        sum_ready = sem("sum_ready")
        center_done = sem("center_done")
        centered_ready = sem("centered_ready")
        squared_ready = sem("squared_ready")
        var_done = sem("var_done")
        std_ready = sem("std_ready")
        rstd_ready = sem("rstd_ready")
        repeated_ready = sem("repeated_ready")
        spread_done = sem("spread_done")
        normed_ready = sem("normed_ready")
        out_stored = [sem(f"out_stored{i}") for i in range(2)]
        last_stored = [sem(f"last_stored{i}") for i in range(2)]

        CONSTS_SET = 7
        N_CONSTS = 16 * (len(WEIGHTS) - 1 + len(BIASES))

        IN_CHUNK = CHUNK // D
        X_FIRST = 2 * CHUNK
        FIRST_SPLITS = 2

        def blocks_of(chunk):
            return bass.ds(chunk * CHUNK, CHUNK)

        def block_of(chunk, j):
            return bass.ds(chunk * CHUNK + j * D, D)

        def block_in(tile, j):
            return tile[:, j * D:(j + 1) * D]

        def loads_of(product, chunk, g):
            passes = g % SLOTS >= SLOTS - KEPT
            per_product = CHUNKS * GROUPS // SLOTS - (1 if passes else 0)
            passed = 1 if passes and not (isinstance(chunk, int) and chunk == 0 and g < GROUPS) else 0
            return product * per_product + (chunk * (GROUPS // SLOTS) + g // SLOTS + 1 - passed)

        def kept_of(chunk, g):
            return kept[g - GROUPS + KEPT] if (isinstance(chunk, int) and chunk == 0
                                               and GROUPS - KEPT <= g < GROUPS) else None

        def split_ahead(split, product, chunk, first, last):
            for g in range(first + LEAD, last + LEAD):
                split((product * CHUNKS + chunk) * GROUPS + g, g % SLOTS,
                      loads_of(product, chunk, g), kept_of(chunk, g))

        block = ctx.enter_context(nc.Block())

        @block.sync
        def _(sp):
            sp.dma_start(w["uv_W1"][:], weights["uv_W1"]).then_inc(x_loaded[0], 16)
            sp.dma_start(resid[:, 0:X_FIRST], x_t[:, 0:X_FIRST]).then_inc(x_loaded[0], 16)

            def load(group, chunk, g):
                if not isinstance(group, int) or group >= SLOTS:
                    sp.wait_ge(low_ready, group - SLOTS + 1)
                sp.dma_start(raw[g % SLOTS][:], adj[chunk, g]).then_inc(raw_loaded[g % SLOTS], 16)

            sp.dma_start(resid[:, X_FIRST:], x_t[:, X_FIRST:]).then_inc(x_loaded[1], 16)
            for g in range(GROUPS - KEPT):
                load(g, 0, g)
            for k in range(KEPT):
                sp.dma_start(kept[k][:], adj[0, GROUPS - KEPT + k]).then_inc(kept_loaded[k], 16)
            with sp.Fori(1, CHUNKS) as c:
                for g in range(GROUPS):
                    load(c * GROUPS + g, bass.ds(c, 1), g)
            with sp.Fori(1, PRODUCTS) as product:
                for g in range(GROUPS - KEPT):
                    load(product * CHUNKS * GROUPS + g, 0, g)
                with sp.Fori(1, CHUNKS) as c:
                    for g in range(GROUPS):
                        load((product * CHUNKS + c) * GROUPS + g, bass.ds(c, 1), g)

            for c in (CHUNKS - 2, CHUNKS - 1):
                sp.wait_ge(normed_ready, CHUNKS + c + 1)
                sp.dma_start(out_t[c], normed[c % 2][:]).then_inc(last_stored[c % 2], 16)
            for i in range(2):
                sp.wait_ge(last_stored[i], 16)

        @block.gpsimd
        def _(pool):
            nc.gpsimd.memset(average[:], 1.0 / D).then_inc(consts_set, 1)
            nc.gpsimd.memset(eps[:], EPS).then_inc(consts_set, 1)
            nc.gpsimd.memset(ones[:], 1.0).then_inc(consts_set, 1)
            nc.gpsimd.memset(identity[:], 0.0).then_inc(consts_set, 1)
            nc.gpsimd.memset(centering[:], -1.0 / D).then_inc(consts_set, 1)
            pool.wait_ge(consts_set, 5)
            for matrix, diagonal_value in ((identity, 1.0), (centering, 1.0 - 1.0 / D)):
                nc.gpsimd.affine_select(out=matrix[:], in_=matrix[:], compare_op=ALU.not_equal,
                                        fill=diagonal_value, base=0, pattern=[[-1, D]],
                                        channel_multiplier=1).then_inc(consts_set, 1)
            for name in WEIGHTS[1:]:
                pool.dma_start(w[name][:], weights[name]).then_inc(consts_loaded, 16)
            for name in BIASES:
                pool.dma_start(b[name][:], biases[name]).then_inc(consts_loaded, 16)
            with pool.Fori(0, CHUNKS - 3, 2) as c:
                for i in range(2):
                    pool.wait_ge(normed_ready, CHUNKS + c + i + 1)
                    pool.dma_start(out_t[bass.ds(c + i, 1)], normed[i][:]).then_inc(out_stored[i], 16)
            for i in range(2):
                pool.wait_ge(out_stored[i], 16 * (CHUNKS // 2 - 1))

        @block.scalar
        def _(act):
            def split(group, slot, loads, kept_tile):
                if kept_tile is None:
                    act.wait_ge(raw_loaded[slot], loads * 16)
                elif isinstance(group, int):
                    act.wait_ge(kept_loaded[kept.index(kept_tile)], 16)
                if not isinstance(group, int) or group >= SLOTS:
                    act.wait_ge(group_used, group - SLOTS + 1)
                source = raw[slot] if kept_tile is None else kept_tile
                nc.scalar.activation(high[slot][:], source[:], ACT.Copy).then_inc(high_ready, 1)

            def project_high(step, chunk, side, parity):
                act.wait_ge(proj_done, CHUNKS + step + 1)
                nc.scalar.activation(p_high[parity][:, blocks_of(chunk)], proj[side][:],
                                     ACT.Copy).then_inc(p_high_ready, 1)

            def first_bias(step, side, way):
                act.wait_ge(group_used, (step + 1) * GROUPS)
                nc.scalar.activation(z[:], acc[side][:], ACT.Identity,
                                     bias=b[f"{way}_b1"][:]).then_inc(z_ready, 1)

            def later_bias(step, k, way):
                act.wait_ge(layer_done, step * 2 + k - 1)
                nc.scalar.activation(z[:], layer[:], ACT.Identity,
                                     bias=b[f"{way}_b{k}"][:]).then_inc(z_ready, 1)

            def squares(n):
                act.wait_ge(center_done, n + 1)
                nc.scalar.activation(squared[:], minus_mean[:], ACT.Square).then_inc(squared_ready, 1)
                nc.scalar.activation(centered[:], minus_mean[:], ACT.Copy).then_inc(centered_ready, 1)

            def deviation(n):
                act.wait_ge(var_done, n + 1)
                nc.scalar.activation(std[:], var[:, 0:IN_CHUNK], ACT.Sqrt, bias=eps[:]).then_inc(std_ready, 1)

            def repeat_deviation(n):
                act.wait_ge(rstd_ready, n + 1)
                for j in range(IN_CHUNK):
                    last = nc.scalar.activation(block_in(repeated, j), ones[:], ACT.Copy,
                                                scale=rstd[:, j:j + 1])
                last.then_inc(repeated_ready, 1)

            def project_norm_high(step, chunk, side):
                act.wait_ge(rstd_ready, step - NORM_STEP + 1)
                act.wait_ge(proj_done, CHUNKS + step + 1)
                for j in range(IN_CHUNK):
                    last = nc.scalar.activation(p_high[1][:, block_of(chunk, j)], block_in(proj[side], j),
                                                ACT.Copy, scale=rstd[:, j:j + 1])
                last.then_inc(p_high_ready, 1)

            def round_tail(step, running, chunk, side, way, parity):
                def ahead(first, last):
                    split_ahead(split, *running, first, last)
                first_bias(step, side, way)
                ahead(0, LAYER_2_AT + 1)
                later_bias(step, 2, way)
                ahead(LAYER_2_AT + 1, LAYER_3_AT + 1)
                later_bias(step, 3, way)
                ahead(LAYER_3_AT + 1, PROJECT_AT + 1)
                project_high(step, chunk, side, parity)
                ahead(PROJECT_AT + 1, GROUPS)

            def norm_tail(step, running, chunk, side):
                n = step - NORM_STEP
                def ahead(first, last):
                    split_ahead(split, *running, first, last)
                first_bias(step, side, "uv")
                ahead(0, NORM_LAYER_2_AT + 1)
                later_bias(step, 2, "uv")
                ahead(NORM_LAYER_2_AT + 1, NORM_LAYER_3_AT + 1)
                later_bias(step, 3, "uv")
                ahead(NORM_LAYER_3_AT + 1, NORM_CENTER_AT + 1)
                squares(n)
                ahead(NORM_CENTER_AT + 1, NORM_VAR_AT + 1)
                deviation(n)
                ahead(NORM_VAR_AT + 1, NORM_PROJECT_AT + 1)
                repeat_deviation(n)
                project_norm_high(step, chunk, side)
                ahead(NORM_PROJECT_AT + 1, GROUPS)

            def last_tail(step, chunk, side, splits):
                n = step - NORM_STEP
                def ahead(first, last):
                    split_ahead(split, PRODUCTS - 1, chunk + 1, first, min(last, splits))
                ahead(0, LAST_CENTER_AT + 1)
                squares(n)
                ahead(LAST_CENTER_AT + 1, LAST_VAR_AT + 1)
                deviation(n)
                ahead(LAST_VAR_AT + 1, LAST_SPREAD_AT)
                repeat_deviation(n)
                ahead(LAST_SPREAD_AT, GROUPS)

            for c in range(CHUNKS):
                project_high(c - CHUNKS, c, c % 2, 0)
                if c >= CHUNKS - 2 * FIRST_SPLITS and c % 2:
                    g = (c + 1 - CHUNKS) // 2 + FIRST_SPLITS - 1
                    split(g, g % SLOTS, loads_of(0, 0, g), kept_of(0, g))
            for g in range(FIRST_SPLITS, GROUPS + LEAD):
                split(g, g % SLOTS, loads_of(0, 0, g), kept_of(0, g))
            act.wait_ge(consts_loaded, N_CONSTS)
            act.wait_ge(consts_set, CONSTS_SET)
            with act.Fori(0, ROUND_TRIPS) as trip:
                for i, way in enumerate(("uv", "vu")):
                    product = trip * 2 + i
                    with act.Fori(0, CHUNKS - 3, 2) as c:
                        for side in range(2):
                            round_tail(product * CHUNKS + c + side, (product, c + side + 1), c + side,
                                       side, way, 1 - i)
                    round_tail(product * CHUNKS + CHUNKS - 2, (product, CHUNKS - 1), CHUNKS - 2, 0, way, 1 - i)
                    round_tail(product * CHUNKS + CHUNKS - 1, (product + 1, 0), CHUNKS - 1, 1, way, 1 - i)
            with act.Fori(0, CHUNKS - 3, 2) as c:
                for side in range(2):
                    norm_tail(NORM_STEP + c + side, (PRODUCTS - 2, c + side + 1), c + side, side)
            norm_tail(LAST_STEP - 2, (PRODUCTS - 2, CHUNKS - 1), CHUNKS - 2, 0)
            norm_tail(LAST_STEP - 1, (PRODUCTS - 1, 0), CHUNKS - 1, 1)
            with act.Fori(0, CHUNKS - 3, 2) as c:
                for side in range(2):
                    last_tail(LAST_STEP + c + side, c + side, side, GROUPS)
            last_tail(STEPS - 2, CHUNKS - 2, 0, GROUPS - LEAD)
            last_tail(STEPS - 1, CHUNKS - 1, 1, 0)

        @block.vector
        def _(dve):
            def split(group, slot, loads, kept_tile):
                dve.wait_ge(high_ready, group + 1)
                if not isinstance(group, int) or group >= SLOTS:
                    dve.wait_ge(group_used, group - SLOTS + 1)
                source = raw[slot] if kept_tile is None else kept_tile
                nc.vector.tensor_tensor(low[slot][:], source[:], high[slot][:].bitcast(F32),
                                        ALU.subtract).then_inc(low_ready, 1)

            def leaky(step, k):
                dve.wait_ge(z_ready, step * 3 + k)
                nc.vector.scalar_tensor_tensor(out=h[:], in0=z[:], scalar=SLOPE, in1=z[:],
                                               op0=ALU.mult, op1=ALU.max).then_inc(h_ready, 1)

            def project_low(step, chunk, side, parity):
                dve.wait_ge(p_high_ready, CHUNKS + step + 1)
                nc.vector.tensor_tensor(p_low[parity][:, blocks_of(chunk)], proj[side][:],
                                        p_high[parity][:, blocks_of(chunk)].bitcast(F32),
                                        ALU.subtract).then_inc(p_low_ready, 1)

            def add_resid(step, chunk):
                dve.wait_ge(h_ready, step * 3 + 3)
                nc.vector.tensor_tensor(h[:], h[:], resid[:, blocks_of(chunk)],
                                        ALU.add).then_inc(sum_ready, 1)

            def add_resid_last(step, chunk, side):
                dve.wait_ge(group_used, (step + 1) * GROUPS)
                nc.vector.tensor_tensor(h[:], acc[side][:], resid[:, blocks_of(chunk)],
                                        ALU.add).then_inc(sum_ready, 1)

            def invert(n):
                dve.wait_ge(std_ready, n + 1)
                nc.vector.reciprocal(rstd[:], std[:]).then_inc(rstd_ready, 1)

            def project_norm_low(step, chunk, side):
                dve.wait_ge(rstd_ready, step - NORM_STEP + 1)
                dve.wait_ge(p_high_ready, CHUNKS + step + 1)
                for j in range(IN_CHUNK):
                    last = nc.vector.scalar_tensor_tensor(
                        out=p_low[1][:, block_of(chunk, j)], in0=block_in(proj[side], j),
                        scalar=rstd[:, j:j + 1], in1=p_high[1][:, block_of(chunk, j)].bitcast(F32),
                        op0=ALU.mult, op1=ALU.subtract)
                last.then_inc(p_low_ready, 1)

            def norm(n, target):
                dve.wait_ge(spread_done, n + 1)
                dve.wait_ge(centered_ready, n + 1)
                nc.vector.tensor_tensor(target, centered[:], spread[:], ALU.mult).then_inc(normed_ready, 1)

            def round_tail(step, running, chunk, side, parity):
                def ahead(first, last):
                    split_ahead(split, *running, first, last)
                leaky(step, 1)
                ahead(0, LAYER_2_AT + 1)
                leaky(step, 2)
                ahead(LAYER_2_AT + 1, LAYER_3_AT + 1)
                leaky(step, 3)
                ahead(LAYER_3_AT + 1, PROJECT_AT + 1)
                project_low(step, chunk, side, parity)
                ahead(PROJECT_AT + 1, GROUPS)

            def norm_tail(step, running, chunk, side):
                n = step - NORM_STEP
                def ahead(first, last):
                    split_ahead(split, *running, first, last)
                leaky(step, 1)
                ahead(0, NORM_LAYER_2_AT + 1)
                leaky(step, 2)
                ahead(NORM_LAYER_2_AT + 1, NORM_LAYER_3_AT + 1)
                leaky(step, 3)
                add_resid(step, chunk)
                ahead(NORM_LAYER_3_AT + 1, NORM_VAR_AT + 1)
                invert(n)
                ahead(NORM_VAR_AT + 1, NORM_PROJECT_AT + 1)
                project_norm_low(step, chunk, side)
                ahead(NORM_PROJECT_AT + 1, NORM_SPREAD_AT + 1)
                norm(n, resid[:, blocks_of(chunk)])
                ahead(NORM_SPREAD_AT + 1, GROUPS)

            def last_tail(step, chunk, side, splits):
                n = step - NORM_STEP
                def ahead(first, last):
                    split_ahead(split, PRODUCTS - 1, chunk + 1, first, min(last, splits))
                add_resid_last(step, chunk, side)
                ahead(0, LAST_VAR_AT + 1)
                invert(n)
                ahead(LAST_VAR_AT + 1, LAST_SPREAD_AT + 1)
                if not isinstance(chunk, int) or chunk >= 2:
                    dve.wait_ge(out_stored[side], (chunk - side) * 8)
                norm(n, normed[side][:])
                ahead(LAST_SPREAD_AT + 1, GROUPS)

            for c in range(CHUNKS):
                project_low(c - CHUNKS, c, c % 2, 0)
                if c >= CHUNKS - 2 * FIRST_SPLITS and c % 2:
                    g = (c + 1 - CHUNKS) // 2 + FIRST_SPLITS - 1
                    split(g, g % SLOTS, loads_of(0, 0, g), kept_of(0, g))
            for g in range(FIRST_SPLITS, GROUPS + LEAD):
                split(g, g % SLOTS, loads_of(0, 0, g), kept_of(0, g))
            with dve.Fori(0, ROUND_TRIPS) as trip:
                for i in range(2):
                    product = trip * 2 + i
                    with dve.Fori(0, CHUNKS - 3, 2) as c:
                        for side in range(2):
                            round_tail(product * CHUNKS + c + side, (product, c + side + 1), c + side,
                                       side, 1 - i)
                    round_tail(product * CHUNKS + CHUNKS - 2, (product, CHUNKS - 1), CHUNKS - 2, 0, 1 - i)
                    round_tail(product * CHUNKS + CHUNKS - 1, (product + 1, 0), CHUNKS - 1, 1, 1 - i)
            with dve.Fori(0, CHUNKS - 3, 2) as c:
                for side in range(2):
                    norm_tail(NORM_STEP + c + side, (PRODUCTS - 2, c + side + 1), c + side, side)
            norm_tail(LAST_STEP - 2, (PRODUCTS - 2, CHUNKS - 1), CHUNKS - 2, 0)
            norm_tail(LAST_STEP - 1, (PRODUCTS - 1, 0), CHUNKS - 1, 1)
            dve.wait_ge(normed_ready, CHUNKS)
            for side in range(2):
                last_tail(LAST_STEP + side, side, side, GROUPS)
            with dve.Fori(2, CHUNKS - 3, 2) as c:
                for side in range(2):
                    last_tail(LAST_STEP + c + side, c + side, side, GROUPS)
            last_tail(STEPS - 2, CHUNKS - 2, 0, GROUPS - LEAD)
            last_tail(STEPS - 1, CHUNKS - 1, 1, 0)

        @block.tensor
        def _(pe):
            def dense(weight, step, k):
                pe.wait_ge(h_ready, step * 3 + k - 1)
                nc.tensor.matmul(layer[:], weight[:], h[:], start=True,
                                 stop=True).then_inc(layer_done, 1)

            def project(step, weight, side, source):
                for j in range(CHUNK // D):
                    last = nc.tensor.matmul(proj[side][:, j * D:(j + 1) * D], source[:, j * D:(j + 1) * D],
                                            weight[:], start=True, stop=True)
                last.then_inc(proj_done, 1)

            def round_project(step, weight, side):
                pe.wait_ge(h_ready, step * 3 + 3)
                pe.wait_ge(p_low_ready, step + CHUNKS - 1)
                project(step, weight, side, h)

            def center(n):
                pe.wait_ge(sum_ready, n + 1)
                nc.tensor.matmul(minus_mean[:], centering[:], h[:], start=True,
                                 stop=True).then_inc(center_done, 1)

            def variance(n):
                pe.wait_ge(squared_ready, n + 1)
                for j in range(IN_CHUNK):
                    last = nc.tensor.matmul(var[:, j:j + 1], block_in(squared, j), average[:],
                                            start=True, stop=True)
                last.then_inc(var_done, 1)

            def norm_project(step, side):
                pe.wait_ge(centered_ready, step - NORM_STEP + 1)
                pe.wait_ge(p_low_ready, step + CHUNKS - 1)
                project(step, w["gcn_W"], side, centered)

            def spread_deviation(n):
                pe.wait_ge(repeated_ready, n + 1)
                for j in range(IN_CHUNK):
                    done = nc.tensor.transpose(block_in(spread, j), block_in(repeated, j), identity[:])
                done.then_inc(spread_done, 1)

            def multiply(step, side, parity, first, last, opens):
                for g in range(first, last):
                    slot = g % SLOTS
                    if opens:
                        pe.wait_ge(p_low_ready, step + g + 1)
                    pe.wait_ge(low_ready, step * GROUPS + g + 1)
                    for j in range(PER_GROUP):
                        at = (g * PER_GROUP + j) * D
                        columns = slice(j * CHUNK, (j + 1) * CHUNK)
                        for i, (part, adj_part) in enumerate(((p_low, high), (p_high, high), (p_high, low))):
                            done = nc.tensor.matmul(
                                acc[side][:], part[parity][:, at:at + D], adj_part[slot][:, columns],
                                start=(g == 0 and j == 0 and i == 0),
                                stop=(g == GROUPS - 1 and j == PER_GROUP - 1 and i == 2))
                    done.then_inc(group_used, 1)

            def round_step(step, side, parity, way, following, opens=False):
                def groups(first, last):
                    multiply(step, side, parity, first, last, opens)
                groups(0, LAYER_2_AT + 1)
                dense(w[f"{way}_W2"], step - 1, 2)
                groups(LAYER_2_AT + 1, LAYER_3_AT + 1)
                dense(w[f"{way}_W3"], step - 1, 3)
                groups(LAYER_3_AT + 1, PROJECT_AT + 1)
                round_project(step - 1, w[f"{following}_W1"], 1 - side)
                groups(PROJECT_AT + 1, GROUPS)

            def norm_step(step, side, parity, opens=False):
                n = step - 1 - NORM_STEP
                def groups(first, last):
                    multiply(step, side, parity, first, last, opens)
                groups(0, NORM_LAYER_2_AT + 1)
                dense(w["uv_W2"], step - 1, 2)
                groups(NORM_LAYER_2_AT + 1, NORM_LAYER_3_AT + 1)
                dense(w["uv_W3"], step - 1, 3)
                groups(NORM_LAYER_3_AT + 1, NORM_CENTER_AT + 1)
                center(n)
                groups(NORM_CENTER_AT + 1, NORM_VAR_AT + 1)
                variance(n)
                groups(NORM_VAR_AT + 1, NORM_PROJECT_AT + 1)
                norm_project(step - 1, 1 - side)
                groups(NORM_PROJECT_AT + 1, NORM_SPREAD_AT + 1)
                spread_deviation(n)
                groups(NORM_SPREAD_AT + 1, GROUPS)

            def last_step(step, side, parity):
                n = step - 1 - NORM_STEP
                def groups(first, last):
                    multiply(step, side, parity, first, last, False)
                groups(0, LAST_CENTER_AT + 1)
                center(n)
                groups(LAST_CENTER_AT + 1, LAST_VAR_AT + 1)
                variance(n)
                groups(LAST_VAR_AT + 1, LAST_SPREAD_AT + 1)
                spread_deviation(n)
                groups(LAST_SPREAD_AT + 1, GROUPS)

            def project_x(c):
                if c >= 2:
                    pe.wait_ge(p_low_ready, c - 1)
                if c * CHUNK == X_FIRST:
                    pe.wait_ge(x_loaded[1], 16)
                project(c - CHUNKS, w["uv_W1"], c % 2, resid[:, c * CHUNK:(c + 1) * CHUNK])

            pe.wait_ge(x_loaded[0], 32)
            for c in range(CHUNKS):
                project_x(c)
            multiply(0, 0, 0, 0, GROUPS, True)
            pe.wait_ge(consts_loaded, N_CONSTS)
            pe.wait_ge(consts_set, CONSTS_SET)

            with pe.Fori(0, ROUND_TRIPS) as trip:
                for i, (way, following) in enumerate((("uv", "vu"), ("vu", "uv"))):
                    start = (trip * 2 + i) * CHUNKS
                    with pe.Fori(1, CHUNKS - 2, 2) as c:
                        round_step(start + c, 1, i, way, following)
                        round_step(start + c + 1, 0, i, way, following)
                    round_step(start + CHUNKS - 1, 1, i, way, following)
                    round_step(start + CHUNKS, 0, 1 - i, way, following, opens=True)
            with pe.Fori(1, CHUNKS - 2, 2) as c:
                norm_step(NORM_STEP + c, 1, 0)
                norm_step(NORM_STEP + c + 1, 0, 0)
            norm_step(NORM_STEP + CHUNKS - 1, 1, 0)
            norm_step(LAST_STEP, 0, 1, opens=True)
            with pe.Fori(1, CHUNKS - 2, 2) as c:
                last_step(LAST_STEP + c, 1, 1)
                last_step(LAST_STEP + c + 1, 0, 1)
            last_step(STEPS - 1, 1, 1)
            n = STEPS - 1 - NORM_STEP
            center(n)
            variance(n)
            spread_deviation(n)


_WEIGHTS = {"uv_W1": "L0_gnn_uv_W1", "uv_W2": "L0_gnn_uv_W2", "uv_W3": "L0_gnn_uv_W3",
            "vu_W1": "L0_gnn_vu_W1", "vu_W2": "L0_gnn_vu_W2", "vu_W3": "L0_gnn_vu_W3",
            "gcn_W": "L1_gnn_weight"}
_BIASES = {"uv_b1": "L0_gnn_uv_b1", "uv_b2": "L0_gnn_uv_b2", "uv_b3": "L0_gnn_uv_b3",
           "vu_b1": "L0_gnn_vu_b1", "vu_b2": "L0_gnn_vu_b2", "vu_b3": "L0_gnn_vu_b3"}


def kernel(**inputs):
    import numpy as _np
    import concourse.bacc as _bacc
    from concourse.bass_utils import run_bass_kernel_spmd as _run

    nc = _bacc.Bacc("TRN2", target_bir_lowering=False, num_devices=1)
    arrays = {}

    def put(name, array):
        arrays[name] = _np.ascontiguousarray(array)
        return nc.dram_tensor(name, arrays[name].shape, F32, kind="ExternalInput").ap()

    adj = _np.asarray(inputs["adj"]).reshape(CHUNKS, CHUNK, GROUPS, PER_GROUP, D)
    adj = put("adj_dram", adj.transpose(0, 2, 4, 3, 1).reshape(CHUNKS, GROUPS, D, GROUP))
    x_t = put("x_t_dram", _np.asarray(inputs["x"]).T)
    weights = {k: put(f"{k}_dram", inputs[v]) for k, v in _WEIGHTS.items()}
    biases = {k: put(f"{k}_dram", _np.asarray(inputs[v]).reshape(D, 1)) for k, v in _BIASES.items()}
    out_t = nc.dram_tensor("out_t_dram", (CHUNKS, D, CHUNK), F32, kind="ExternalOutput").ap()
    gnn_kernel(nc, adj, x_t, weights, biases, out_t)
    r = _run(nc, [arrays], core_ids=[0])
    got = r.results[0]["out_t_dram"]
    return _np.ascontiguousarray(got.transpose(0, 2, 1).reshape(N, D))
```
